# Optimizing a Trainium2 kernel written in Bass

```python
import numpy as np
import jax
import jax.numpy as jnp

def _softmax(x, axis=-1):
    return jax.nn.softmax(x, axis=axis)

def _gelu(x):
    return jax.nn.gelu(x, approximate=True)

def _silu(x):
    return jax.nn.silu(x)

def _sigmoid(x):
    return jax.nn.sigmoid(x)

def _layernorm(x, axis=-1, eps=1e-05):
    m = jnp.mean(x, axis=axis, keepdims=True)
    v = jnp.var(x, axis=axis, keepdims=True)
    return (x - m) / jnp.sqrt(v + eps)

def _scatter_add(tgt, idx, src, axis=0):
    return tgt.at[idx].add(src)

def _segment_sum(src, seg, n):
    return jax.ops.segment_sum(src, seg, n)
kernel_name = 'mk_rec_standalone_d1_rec_r8_5c6e7b'

def setup_inputs(seed: int=0):
    np.random.seed(seed)
    _w = jnp.asarray

    def _rec_inputs():
        import jax
        import jax.numpy as jnp
        _rk = jax.random.key(seed)
        r_x = jnp.stack([jax.random.randint(jax.random.fold_in(jax.random.fold_in(_rk, 1), 0), (2048,), 8, 4992, jnp.int32), jax.random.randint(jax.random.fold_in(jax.random.fold_in(_rk, 1), 1), (2048,), 138, 40001, jnp.int32), jax.random.randint(jax.random.fold_in(jax.random.fold_in(_rk, 1), 2), (2048,), 9, 39986, jnp.int32), jax.random.randint(jax.random.fold_in(jax.random.fold_in(_rk, 1), 3), (2048,), 140, 39909, jnp.int32), jax.random.randint(jax.random.fold_in(jax.random.fold_in(_rk, 1), 4), (2048,), 46, 39997, jnp.int32), jax.random.randint(jax.random.fold_in(jax.random.fold_in(_rk, 1), 5), (2048,), 73, 39997, jnp.int32), jax.random.randint(jax.random.fold_in(jax.random.fold_in(_rk, 1), 6), (2048,), 49, 39958, jnp.int32), jax.random.randint(jax.random.fold_in(jax.random.fold_in(_rk, 1), 7), (2048,), 4, 39877, jnp.int32), jax.random.randint(jax.random.fold_in(jax.random.fold_in(_rk, 1), 8), (2048,), 36, 39950, jnp.int32), jax.random.randint(jax.random.fold_in(jax.random.fold_in(_rk, 1), 9), (2048,), 10, 39885, jnp.int32), jax.random.randint(jax.random.fold_in(jax.random.fold_in(_rk, 1), 10), (2048,), 24, 39999, jnp.int32), jax.random.randint(jax.random.fold_in(jax.random.fold_in(_rk, 1), 11), (2048,), 47, 39985, jnp.int32), jax.random.randint(jax.random.fold_in(jax.random.fold_in(_rk, 1), 12), (2048,), 60, 39917, jnp.int32), jax.random.randint(jax.random.fold_in(jax.random.fold_in(_rk, 1), 13), (2048,), 60, 39998, jnp.int32), jax.random.randint(jax.random.fold_in(jax.random.fold_in(_rk, 1), 14), (2048,), 14, 39940, jnp.int32), jax.random.randint(jax.random.fold_in(jax.random.fold_in(_rk, 1), 15), (2048,), 71, 39977, jnp.int32), jax.random.randint(jax.random.fold_in(jax.random.fold_in(_rk, 1), 16), (2048,), 103, 39989, jnp.int32), jax.random.randint(jax.random.fold_in(jax.random.fold_in(_rk, 1), 17), (2048,), 2, 39995, jnp.int32), jax.random.randint(jax.random.fold_in(jax.random.fold_in(_rk, 1), 18), (2048,), 94, 39954, jnp.int32), jax.random.randint(jax.random.fold_in(jax.random.fold_in(_rk, 1), 19), (2048,), 70, 39990, jnp.int32), jax.random.randint(jax.random.fold_in(jax.random.fold_in(_rk, 1), 20), (2048,), 27, 39993, jnp.int32), jax.random.randint(jax.random.fold_in(jax.random.fold_in(_rk, 1), 21), (2048,), 0, 39970, jnp.int32), jax.random.randint(jax.random.fold_in(jax.random.fold_in(_rk, 1), 22), (2048,), 94, 40001, jnp.int32), jax.random.randint(jax.random.fold_in(jax.random.fold_in(_rk, 1), 23), (2048,), 17, 39986, jnp.int32), jax.random.randint(jax.random.fold_in(jax.random.fold_in(_rk, 1), 24), (2048,), 38, 39995, jnp.int32), jax.random.randint(jax.random.fold_in(jax.random.fold_in(_rk, 1), 25), (2048,), 7, 40001, jnp.int32), jax.random.randint(jax.random.fold_in(jax.random.fold_in(_rk, 1), 26), (2048,), 18, 39962, jnp.int32), jax.random.randint(jax.random.fold_in(jax.random.fold_in(_rk, 1), 27), (2048,), 20, 39979, jnp.int32), jax.random.randint(jax.random.fold_in(jax.random.fold_in(_rk, 1), 28), (2048,), 11, 4998, jnp.int32), jax.random.randint(jax.random.fold_in(jax.random.fold_in(_rk, 1), 29), (2048,), 49, 39977, jnp.int32), jax.random.randint(jax.random.fold_in(jax.random.fold_in(_rk, 1), 30), (2048,), 3, 4991, jnp.int32), jax.random.randint(jax.random.fold_in(jax.random.fold_in(_rk, 1), 31), (2048,), 12, 39945, jnp.int32), jax.random.randint(jax.random.fold_in(jax.random.fold_in(_rk, 1), 32), (2048,), 47, 4995, jnp.int32), jax.random.randint(jax.random.fold_in(jax.random.fold_in(_rk, 1), 33), (2048,), 14, 39985, jnp.int32), jax.random.randint(jax.random.fold_in(jax.random.fold_in(_rk, 1), 34), (2048,), 165, 39881, jnp.int32), jax.random.randint(jax.random.fold_in(jax.random.fold_in(_rk, 1), 35), (2048,), 73, 39988, jnp.int32), jax.random.randint(jax.random.fold_in(jax.random.fold_in(_rk, 1), 36), (2048,), 22, 39949, jnp.int32), jax.random.randint(jax.random.fold_in(jax.random.fold_in(_rk, 1), 37), (2048,), 22, 39997, jnp.int32), jax.random.randint(jax.random.fold_in(jax.random.fold_in(_rk, 1), 38), (2048,), 15, 39877, jnp.int32), jax.random.randint(jax.random.fold_in(jax.random.fold_in(_rk, 1), 39), (2048,), 1, 39991, jnp.int32), jax.random.randint(jax.random.fold_in(jax.random.fold_in(_rk, 1), 40), (2048,), 70, 39853, jnp.int32), jax.random.randint(jax.random.fold_in(jax.random.fold_in(_rk, 1), 41), (2048,), 11, 4999, jnp.int32), jax.random.randint(jax.random.fold_in(jax.random.fold_in(_rk, 1), 42), (2048,), 164, 39998, jnp.int32), jax.random.randint(jax.random.fold_in(jax.random.fold_in(_rk, 1), 43), (2048,), 67, 39857, jnp.int32), jax.random.randint(jax.random.fold_in(jax.random.fold_in(_rk, 1), 44), (2048,), 7, 39999, jnp.int32), jax.random.randint(jax.random.fold_in(jax.random.fold_in(_rk, 1), 45), (2048,), 61, 39929, jnp.int32), jax.random.randint(jax.random.fold_in(jax.random.fold_in(_rk, 1), 46), (2048,), 0, 39986, jnp.int32), jax.random.randint(jax.random.fold_in(jax.random.fold_in(_rk, 1), 47), (2048,), 15, 4999, jnp.int32), jax.random.randint(jax.random.fold_in(jax.random.fold_in(_rk, 1), 48), (2048,), 80, 4989, jnp.int32), jax.random.randint(jax.random.fold_in(jax.random.fold_in(_rk, 1), 49), (2048,), 69, 39999, jnp.int32), jax.random.randint(jax.random.fold_in(jax.random.fold_in(_rk, 1), 50), (2048,), 113, 39998, jnp.int32), jax.random.randint(jax.random.fold_in(jax.random.fold_in(_rk, 1), 51), (2048,), 110, 39911, jnp.int32), jax.random.randint(jax.random.fold_in(jax.random.fold_in(_rk, 1), 52), (2048,), 36, 39989, jnp.int32), jax.random.randint(jax.random.fold_in(jax.random.fold_in(_rk, 1), 53), (2048,), 24, 39998, jnp.int32), jax.random.randint(jax.random.fold_in(jax.random.fold_in(_rk, 1), 54), (2048,), 25, 39946, jnp.int32), jax.random.randint(jax.random.fold_in(jax.random.fold_in(_rk, 1), 55), (2048,), 50, 40001, jnp.int32), jax.random.randint(jax.random.fold_in(jax.random.fold_in(_rk, 1), 56), (2048,), 42, 39958, jnp.int32), jax.random.randint(jax.random.fold_in(jax.random.fold_in(_rk, 1), 57), (2048,), 45, 39978, jnp.int32), jax.random.randint(jax.random.fold_in(jax.random.fold_in(_rk, 1), 58), (2048,), 49, 39983, jnp.int32), jax.random.randint(jax.random.fold_in(jax.random.fold_in(_rk, 1), 59), (2048,), 28, 39996, jnp.int32), jax.random.randint(jax.random.fold_in(jax.random.fold_in(_rk, 1), 60), (2048,), 30, 5000, jnp.int32), jax.random.randint(jax.random.fold_in(jax.random.fold_in(_rk, 1), 61), (2048,), 28, 39947, jnp.int32), jax.random.randint(jax.random.fold_in(jax.random.fold_in(_rk, 1), 62), (2048,), 24, 39973, jnp.int32), jax.random.randint(jax.random.fold_in(jax.random.fold_in(_rk, 1), 63), (2048,), 5, 39983, jnp.int32), jax.random.randint(jax.random.fold_in(jax.random.fold_in(_rk, 1), 64), (2048,), 12, 39940, jnp.int32), jax.random.randint(jax.random.fold_in(jax.random.fold_in(_rk, 1), 65), (2048,), 72, 39998, jnp.int32), jax.random.randint(jax.random.fold_in(jax.random.fold_in(_rk, 1), 66), (2048,), 10, 39991, jnp.int32), jax.random.randint(jax.random.fold_in(jax.random.fold_in(_rk, 1), 67), (2048,), 5, 4993, jnp.int32), jax.random.randint(jax.random.fold_in(jax.random.fold_in(_rk, 1), 68), (2048,), 3, 39993, jnp.int32), jax.random.randint(jax.random.fold_in(jax.random.fold_in(_rk, 1), 69), (2048,), 9, 39966, jnp.int32), jax.random.randint(jax.random.fold_in(jax.random.fold_in(_rk, 1), 70), (2048,), 35, 39986, jnp.int32), jax.random.randint(jax.random.fold_in(jax.random.fold_in(_rk, 1), 71), (2048,), 0, 39997, jnp.int32), jax.random.randint(jax.random.fold_in(jax.random.fold_in(_rk, 1), 72), (2048,), 10, 39951, jnp.int32), jax.random.randint(jax.random.fold_in(jax.random.fold_in(_rk, 1), 73), (2048,), 3, 4988, jnp.int32), jax.random.randint(jax.random.fold_in(jax.random.fold_in(_rk, 1), 74), (2048,), 13, 39857, jnp.int32), jax.random.randint(jax.random.fold_in(jax.random.fold_in(_rk, 1), 75), (2048,), 40, 39921, jnp.int32), jax.random.randint(jax.random.fold_in(jax.random.fold_in(_rk, 1), 76), (2048,), 17, 39957, jnp.int32), jax.random.randint(jax.random.fold_in(jax.random.fold_in(_rk, 1), 77), (2048,), 19, 39996, jnp.int32), jax.random.randint(jax.random.fold_in(jax.random.fold_in(_rk, 1), 78), (2048,), 32, 4996, jnp.int32), jax.random.randint(jax.random.fold_in(jax.random.fold_in(_rk, 1), 79), (2048,), 32, 39930, jnp.int32), jax.random.randint(jax.random.fold_in(jax.random.fold_in(_rk, 1), 80), (2048,), 78, 39980, jnp.int32), jax.random.randint(jax.random.fold_in(jax.random.fold_in(_rk, 1), 81), (2048,), 7, 39921, jnp.int32), jax.random.randint(jax.random.fold_in(jax.random.fold_in(_rk, 1), 82), (2048,), 39, 39957, jnp.int32), jax.random.randint(jax.random.fold_in(jax.random.fold_in(_rk, 1), 83), (2048,), 29, 39953, jnp.int32), jax.random.randint(jax.random.fold_in(jax.random.fold_in(_rk, 1), 84), (2048,), 2, 39861, jnp.int32), jax.random.randint(jax.random.fold_in(jax.random.fold_in(_rk, 1), 85), (2048,), 33, 39916, jnp.int32), jax.random.randint(jax.random.fold_in(jax.random.fold_in(_rk, 1), 86), (2048,), 76, 39910, jnp.int32), jax.random.randint(jax.random.fold_in(jax.random.fold_in(_rk, 1), 87), (2048,), 9, 39828, jnp.int32), jax.random.randint(jax.random.fold_in(jax.random.fold_in(_rk, 1), 88), (2048,), 74, 4998, jnp.int32), jax.random.randint(jax.random.fold_in(jax.random.fold_in(_rk, 1), 89), (2048,), 30, 4991, jnp.int32), jax.random.randint(jax.random.fold_in(jax.random.fold_in(_rk, 1), 90), (2048,), 82, 39965, jnp.int32), jax.random.randint(jax.random.fold_in(jax.random.fold_in(_rk, 1), 91), (2048,), 19, 39979, jnp.int32), jax.random.randint(jax.random.fold_in(jax.random.fold_in(_rk, 1), 92), (2048,), 17, 39999, jnp.int32), jax.random.randint(jax.random.fold_in(jax.random.fold_in(_rk, 1), 93), (2048,), 5, 39971, jnp.int32), jax.random.randint(jax.random.fold_in(jax.random.fold_in(_rk, 1), 94), (2048,), 39, 39930, jnp.int32), jax.random.randint(jax.random.fold_in(jax.random.fold_in(_rk, 1), 95), (2048,), 10, 40001, jnp.int32), jax.random.randint(jax.random.fold_in(jax.random.fold_in(_rk, 1), 96), (2048,), 77, 39930, jnp.int32), jax.random.randint(jax.random.fold_in(jax.random.fold_in(_rk, 1), 97), (2048,), 88, 39930, jnp.int32), jax.random.randint(jax.random.fold_in(jax.random.fold_in(_rk, 1), 98), (2048,), 0, 39969, jnp.int32), jax.random.randint(jax.random.fold_in(jax.random.fold_in(_rk, 1), 99), (2048,), 3, 39988, jnp.int32)], axis=1)
        return r_x
    r_x = _rec_inputs()

    def _L0_rec_setup():
        import jax, jax.numpy as jnp
        import numpy as np
        B, M, N, D, C = (1024, 100, 5000, 256, 625)
        key = jax.random.key(seed)
        ks = jax.random.split(key, 5)
        x = jax.random.randint(ks[0], (B, M), 0, N + 1)
        s1 = 1.0 / np.sqrt(N).astype(np.float32)
        W1 = jax.random.uniform(ks[1], (D, N), minval=-s1, maxval=s1, dtype=jnp.float32)
        b1 = jax.random.uniform(ks[2], (D,), minval=-s1, maxval=s1, dtype=jnp.float32)
        s2 = 1.0 / np.sqrt(D).astype(np.float32)
        W2 = jax.random.uniform(ks[3], (C, D), minval=-s2, maxval=s2, dtype=jnp.float32)
        b2 = jax.random.uniform(ks[4], (C,), minval=-s2, maxval=s2, dtype=jnp.float32)
        return {'x': x, 'W1': W1, 'b1': b1, 'W2': W2, 'b2': b2}
    _L0_rec_all = _L0_rec_setup()
    _L0_rec_in = {k: v for k, v in _L0_rec_all.items() if k in ('W1', 'b1', 'W2', 'b2')}
    del _L0_rec_all
    return {'r_x': r_x, 'L0_rec_W1': _L0_rec_in['W1'], 'L0_rec_b1': _L0_rec_in['b1'], 'L0_rec_W2': _L0_rec_in['W2'], 'L0_rec_b2': _L0_rec_in['b2']}

def reference(r_x, L0_rec_W1, L0_rec_b1, L0_rec_W2, L0_rec_b2):
    import jax
    import jax.numpy as jnp

    def _L0_rec_ref(x, W1, b1, W2, b2):
        import jax, jax.numpy as jnp
        import numpy as np
        B, M, N, D, C = (1024, 100, 5000, 256, 625)
        b, n = (x.shape[0], W1.shape[1])
        bipr = jnp.zeros((b, n + 1), jnp.float32)
        bipr = bipr.at[jnp.arange(b)[:, None], x].set(1.0)
        bipr = bipr[:, :-1]
        h = bipr @ W1.T + b1
        return h @ W2.T + b2
    y = _L0_rec_ref(r_x, L0_rec_W1, L0_rec_b1, L0_rec_W2, L0_rec_b2)
    return y

_drawn_inputs = setup_inputs


def setup_inputs(seed=0):
    import zlib

    import numpy as np

    out = dict(_drawn_inputs(seed))
    spreads = {}
    factors = {}
    for name, (base, spread) in spreads.items():
        noise = np.random.default_rng([zlib.crc32(name.encode()), seed]).standard_normal(out[name].shape)
        drawn = base * np.exp(spread * noise) if base else spread * noise
        out[name] = jnp.asarray(drawn.astype(out[name].dtype))
    for name, factor in factors.items():
        out[name] = (out[name] * factor).astype(out[name].dtype)
    return out
```

```python
import concourse.bass as bass
from concourse import mybir
from contextlib import ExitStack


def bag_mlp_kernel(nc: bass.Bass, x_t: bass.AP, w1_t: bass.AP, b1: bass.AP, w2_t: bass.AP, b2: bass.AP,
                   out: bass.AP):
    fp32, f32r = mybir.dt.float32, mybir.dt.float32r
    i32, fp8 = mybir.dt.int32, mybir.dt.float8e4
    ALU = mybir.AluOpType
    ACT = mybir.ActivationFunctionType

    P = 128
    M, ROWS = x_t.shape
    N, D = w1_t.shape
    C = w2_t.shape[1]
    NT = ROWS // P
    KT = -(-N // P)
    TAIL = N - (KT - 1) * P
    DC = D // P
    DROPPED = N

    ONE_BITS = 0x42600000
    STEP_BITS = 0x0C000000
    LO_WORDS = P // 4
    HI_WORDS = KT // 4
    WORDS = LO_WORDS + HI_WORDS

    GROUPS = 8
    GR = P // GROUPS
    CW = 64
    KG = KT // GROUPS
    WCH = KG
    NWCH = KT // WCH
    STAGES = 3
    CS = [0, (C + 1) // 2, C]
    HT_COL = 320

    ctx = ExitStack()
    with ctx:
        def sb(name, shape, dt):
            return ctx.enter_context(nc.sbuf_tensor(name, shape, dt))

        def sem(name):
            return ctx.enter_context(nc.semaphore(name))

        w1_parts = sb("w1_parts", [P, KT, 2, D], f32r)
        w1_stage = sb("w1_stage", [P, STAGES, WCH, D], fp32)
        hits = sb("hits", [P, 2, KT, P], f32r)
        onehot = sb("onehot", [P, 2, P, WORDS], i32)
        x_sb = sb("x_sb", [P, ROWS], i32)
        x_clamped = sb("x_clamped", [P, P], i32)
        x_wrap = sb("x_wrap", [P, P], i32)
        x_index = sb("x_index", [P, P], i32)
        lo_key = sb("lo_key", [P, P], i32)
        hi_key = sb("hi_key", [P, P], i32)
        lo_bits = sb("lo_bits", [P, P], i32)
        hi_bits = sb("hi_bits", [P, P], i32)
        w2_sb = sb("w2_sb", [P, DC, C], fp32)
        b1_sb = sb("b1_sb", [P, DC], fp32)
        b2_sb = sb("b2_sb", [P, C], fp32)
        ident = sb("ident", [P, P], fp32)
        h_high = sb("h_high", [P, D], fp32)
        h_sb = sb("h_sb", [P, D], fp32)
        ht_sb = sb("ht_sb", [P, DC, P], fp32)
        y_sb = sb("y_sb", [P, 2, C], fp32)

        counts = ctx.enter_context(nc.psum_tensor("counts", [P, 2, GR, CW], fp32))
        h_ps = ctx.enter_context(nc.psum_tensor("h_ps", [P, 2, 2 * D], fp32))
        y_ps = ctx.enter_context(nc.psum_tensor("y_ps", [P, 2, 512], fp32))

        x_landed = [sem("x_first_landed"), sem("x_rest_landed")]
        w_landed = [sem(f"w_landed{s}") for s in range(STAGES)]
        tail_zeroed = sem("tail_zeroed")
        small_landed = sem("small_landed")
        ident_made = sem("ident_made")
        w_high = sem("w_high")
        w_ready = sem("w_ready")
        prep = sem("prep")
        onehot_ready = sem("onehot_ready")
        counted = sem("counted")
        hit_ready = sem("hit_ready")
        first_done = sem("first_done")
        high_copied = sem("high_copied")
        h_ready = sem("h_ready")
        ht_done = sem("ht_done")
        ht_ready = sem("ht_ready")
        y_done = sem("y_done")
        y_ready = sem("y_ready")
        stored = [sem("stored0"), sem("stored1")]

        onehot8 = onehot[:, :, :, :].bitcast(fp8)

        block = ctx.enter_context(nc.Block())

        @block.sync
        def _(sp):
            sp.dma_start(x_sb[0:M, 0:P], x_t[:, 0:P]).then_inc(x_landed[0], 16)
            for c in range(NWCH):
                s = c % STAGES
                if c >= STAGES:
                    sp.wait_ge(w_ready, c - STAGES + 1)
                k0 = c * WCH
                full = WCH if c < NWCH - 1 else WCH - 1
                src = w1_t[k0 * P:(k0 + full) * P, :].rearrange("(k p) d -> p k d", p=P)
                sp.dma_start(w1_stage[:, s, 0:full, :], src).then_inc(w_landed[s], 16)
                if c == NWCH - 1:
                    sp.wait_ge(tail_zeroed, 1)
                    sp.dma_start(w1_stage[0:TAIL, s, full, :], w1_t[(KT - 1) * P:N, :]).then_inc(w_landed[s], 16)
                if c == 0:
                    sp.dma_start(x_sb[0:M, P:ROWS], x_t[:, P:ROWS]).then_inc(x_landed[1], 16)
                if c == STAGES - 1:
                    sp.dma_start(w2_sb[:, :, :], w2_t.rearrange("(c p) n -> p c n", p=P)).then_inc(small_landed, 16)
                    sp.dma_start(b1_sb[:, :], b1).then_inc(small_landed, 16)
                    sp.dma_start(b2_sb[:, :], b2.rearrange("(a n) -> a n", a=1).broadcast_to([P, C])).then_inc(small_landed, 16)
            with sp.Fori(0, NT // 2) as i:
                for s in range(2):
                    sp.wait_ge(y_ready, 2 * i + s + 1)
                    sp.dma_start(out[bass.ds((2 * i + s) * P, P), :], y_sb[:, s, :]).then_inc(stored[s], 16)
            for s in range(2):
                sp.wait_ge(stored[s], 16 * (NT // 2))

        @block.gpsimd
        def _(pool):
            nc.gpsimd.memset(ident[:, :], 0.0).then_inc(ident_made, 1)
            pool.wait_ge(ident_made, 1)
            nc.gpsimd.affine_select(out=ident[:, :], in_=ident[:, :], compare_op=ALU.not_equal, fill=1.0,
                                    base=0, pattern=[[-1, P]], channel_multiplier=1).then_inc(ident_made, 1)
            pool.wait_ge(w_ready, NWCH - STAGES)
            nc.gpsimd.memset(w1_stage[:, (NWCH - 1) % STAGES, WCH - 1, :], 0.0).then_inc(tail_zeroed, 1)

        def w_arrived(eng, c):
            eng.wait_ge(w_landed[c % STAGES], 16 * (c // STAGES + 1 + (c == NWCH - 1)))

        @block.scalar
        def _(act):
            def split_high(c):
                w_arrived(act, c)
                nc.scalar.activation(w1_parts[:, c * WCH:(c + 1) * WCH, 0, :], w1_stage[:, c % STAGES, :, :],
                                     ACT.Copy).then_inc(w_high, 1)

            def make_hits(t, par, g):
                act.wait_ge(counted, t * GROUPS + g + 1)
                nc.scalar.activation(hits[:, par, :, g * GR:(g + 1) * GR],
                                     counts[:, g % 2, :, 0:KT].rearrange("p r k -> p k r"),
                                     ACT.Sign).then_inc(hit_ready, 1)

            def copy_high(t, par):
                act.wait_ge(first_done, t + 1)
                act.wait_ge(h_ready, t)
                nc.scalar.activation(h_high[:, :], h_ps[:, par, 0:D], ACT.Copy).then_inc(high_copied, 1)

            def add_b1(t):
                act.wait_ge(ht_done, t + 1)
                for c in range(DC):
                    nc.scalar.activation(ht_sb[:, c, :], y_ps[:, c, HT_COL:HT_COL + P], ACT.Identity,
                                         bias=b1_sb[:, c:c + 1]).then_inc(ht_ready, 1)

            def tile(t, par, first=False, last=False):
                for g in range(GROUPS):
                    if first:
                        split_high(g)
                    if g == 0 and not last:
                        if not first:
                            act.wait_ge(first_done, t)
                    if g == 0 and not first:
                        copy_high(t - 1, 1 - par)
                    if not last:
                        make_hits(t + 1, 1 - par, g)
                    if g == 4 and not first:
                        add_b1(t - 1)

            for g in range(GROUPS):
                make_hits(0, 0, g)
            tile(0, 0, first=True)
            act.wait_ge(small_landed, 48)
            with act.Fori(0, (NT - 2) // 2) as i:
                tile(2 * i + 1, 1)
                tile(2 * i + 2, 0)
            tile(NT - 1, (NT - 1) % 2, last=True)
            copy_high(NT - 1, (NT - 1) % 2)
            add_b1(NT - 1)

        @block.vector
        def _(dve):
            steps = 9

            def keys(t):
                n = [0]

                def step(ins):
                    n[0] += 1
                    ins.then_inc(prep, 1)

                def sofar():
                    dve.wait_ge(prep, steps * t + n[0])

                sl = x_sb[0:M, bass.ds(t * P, P)]
                step(nc.vector.tensor_scalar(x_clamped[0:M, :], sl, -8192.0, 8191.0, ALU.max, ALU.min))
                sofar()
                step(nc.vector.tensor_scalar(x_wrap[0:M, :], x_clamped[0:M, :], 0.0, float(DROPPED + 1),
                                             ALU.is_lt, ALU.mult))
                sofar()
                step(nc.vector.scalar_tensor_tensor(x_index[0:M, :], x_clamped[0:M, :], 0.0, x_wrap[0:M, :],
                                                    ALU.add, ALU.add))
                sofar()
                step(nc.vector.tensor_scalar(lo_bits[0:M, :], x_index[0:M, :], 26, STEP_BITS,
                                             ALU.logical_shift_left, ALU.bitwise_and))
                step(nc.vector.tensor_scalar(hi_bits[0:M, :], x_index[0:M, :], 19, STEP_BITS,
                                             ALU.logical_shift_left, ALU.bitwise_and))
                step(nc.vector.tensor_scalar(lo_key[0:M, :], x_index[0:M, :], P - 4, None, ALU.bitwise_and))
                step(nc.vector.tensor_scalar(hi_key[0:M, :], x_index[0:M, :], -4 * P, None, ALU.bitwise_and))
                sofar()
                step(nc.vector.tensor_scalar(lo_bits[0:M, :], lo_bits[0:M, :], ONE_BITS, None, ALU.bitwise_or))
                step(nc.vector.tensor_scalar(hi_bits[0:M, :], hi_bits[0:M, :], ONE_BITS, None, ALU.bitwise_or))
                sofar()
                assert n[0] == steps

            def encode(t, par, before=None):
                keys(t)
                if before is not None:
                    dve.wait_ge(counted, before)
                for w in range(WORDS):
                    lo = w < LO_WORDS
                    key, bits = (lo_key, lo_bits) if lo else (hi_key, hi_bits)
                    value = 4 * w if lo else 4 * P * (w - LO_WORDS)
                    last = nc.vector.scalar_tensor_tensor(onehot[0:M, par, :, w], key[0:M, :], float(value),
                                                          bits[0:M, :].bitcast(fp32), ALU.is_equal, ALU.mult)
                last.then_inc(onehot_ready, 1)

            def split_low(c):
                w_arrived(dve, c)
                dve.wait_ge(w_high, c + 1)
                nc.vector.tensor_tensor(w1_parts[:, c * WCH:(c + 1) * WCH, 1, :], w1_stage[:, c % STAGES, :, :],
                                        w1_parts[:, c * WCH:(c + 1) * WCH, 0, :].bitcast(fp32),
                                        ALU.subtract).then_inc(w_ready, 1)

            def add_parts(t, par):
                dve.wait_ge(high_copied, t + 1)
                dve.wait_ge(ht_done, t)
                nc.vector.tensor_tensor(h_sb[:, :], h_ps[:, par, D:2 * D], h_high[:, :], ALU.add).then_inc(h_ready, 1)

            def add_b2(t, par, stores=None):
                dve.wait_ge(y_done, t + 1)
                if stores is not None:
                    dve.wait_ge(stored[par], stores)
                for c in range(2):
                    last = nc.vector.tensor_tensor(y_sb[:, par, CS[c]:CS[c + 1]], y_ps[:, c, 0:CS[c + 1] - CS[c]],
                                                   b2_sb[:, CS[c]:CS[c + 1]], ALU.add)
                last.then_inc(y_ready, 1)

            dve.wait_ge(x_landed[0], 16)
            encode(0, 0)
            dve.wait_ge(x_landed[1], 16)
            encode(1, 1)
            for c in range(NWCH):
                split_low(c)
            dve.wait_ge(small_landed, 48)
            encode(2, 0, before=GROUPS)
            add_parts(0, 0)
            encode(3, 1, before=2 * GROUPS)
            add_b2(0, 0)
            add_parts(1, 1)
            encode(4, 0, before=3 * GROUPS)
            add_b2(1, 1)
            with dve.Fori(1, (NT - 4) // 2) as i:
                for par, t in ((0, 2 * i), (1, 2 * i + 1)):
                    add_parts(t, par)
                    encode(t + 3, 1 - par, before=(t + 2) * GROUPS)
                    add_b2(t, par, stores=16 * i)
            for t in range(NT - 4, NT):
                add_parts(t, t % 2)
                if t + 3 < NT:
                    encode(t + 3, 1 - t % 2, before=(t + 2) * GROUPS)
                add_b2(t, t % 2, stores=16 * (t // 2))

        @block.tensor
        def _(pe):
            def count(par, g):
                for r in range(GR):
                    row = g * GR + r
                    last = nc.tensor.matmul(counts[:, g % 2, r, 0:KT], onehot8[0:M, par, row, 0:P],
                                            onehot8[0:M, par, row, P:P + KT], start=True, stop=True)
                last.then_inc(counted, 1)

            def first_layer(par, g):
                for k in range(g * KG, (g + 1) * KG):
                    last = nc.tensor.matmul(h_ps[:, par, :], hits[:, par, k, :],
                                            w1_parts[:, k, :, :].rearrange("p a d -> p (a d)"),
                                            start=(k == 0), stop=(k == KT - 1))
                if g == GROUPS - 1:
                    last.then_inc(first_done, 1)

            def transposes(t):
                pe.wait_ge(h_ready, t + 1)
                if not isinstance(t, int) or t > 0:
                    pe.wait_ge(y_ready, t)
                for c in range(DC):
                    last = nc.tensor.transpose(y_ps[:, c, HT_COL:HT_COL + P], h_sb[:, c * P:(c + 1) * P], ident[:, :])
                last.then_inc(ht_done, 1)

            def second_layer(t):
                pe.wait_ge(ht_ready, DC * (t + 1))
                for b in range(2):
                    for c in range(DC):
                        last = nc.tensor.matmul(y_ps[:, b, 0:CS[b + 1] - CS[b]], ht_sb[:, c, :],
                                                w2_sb[:, c, CS[b]:CS[b + 1]], start=(c == 0), stop=(c == DC - 1))
                last.then_inc(y_done, 1)

            def tile(t, par, first=False, last=False):
                for g in range(GROUPS):
                    if g == 0:
                        pe.wait_ge(hit_ready, (t + 1) * GROUPS)
                        if not last:
                            pe.wait_ge(onehot_ready, t + 2)
                        if not first:
                            pe.wait_ge(h_ready, t - 1)
                    elif g >= 2 and not last:
                        pe.wait_ge(hit_ready, (t + 1) * GROUPS + g - 1)
                    if first:
                        pe.wait_ge(w_ready, g + 1)
                    first_layer(par, g)
                    if not last:
                        count(1 - par, g)
                    if not first:
                        if g == 3:
                            transposes(t - 1)
                        if g == GROUPS - 1:
                            second_layer(t - 1)

            pe.wait_ge(onehot_ready, 1)
            for g in range(GROUPS):
                if g >= 2:
                    pe.wait_ge(hit_ready, g - 1)
                count(0, g)
            pe.wait_ge(ident_made, 2)
            tile(0, 0, first=True)
            with pe.Fori(0, (NT - 2) // 2) as i:
                tile(2 * i + 1, 1)
                tile(2 * i + 2, 0)
            tile(NT - 1, (NT - 1) % 2, last=True)
            transposes(NT - 1)
            second_layer(NT - 1)


def kernel(r_x, L0_rec_W1, L0_rec_b1, L0_rec_W2, L0_rec_b2):
    import numpy as np
    import concourse.bacc as bacc
    from concourse import mybir as mb
    from concourse.bass_utils import run_bass_kernel_spmd

    arrays = {
        "x_t": np.ascontiguousarray(np.asarray(r_x).T),
        "w1_t": np.ascontiguousarray(np.asarray(L0_rec_W1).T),
        "b1": np.ascontiguousarray(np.asarray(L0_rec_b1).reshape(-1, 128).T),
        "w2_t": np.ascontiguousarray(np.asarray(L0_rec_W2).T),
        "b2": np.ascontiguousarray(L0_rec_b2),
    }
    rows, width = arrays["x_t"].shape[1], arrays["w2_t"].shape[1]
    nc = bacc.Bacc("TRN2", target_bir_lowering=False, num_devices=1)
    args = [nc.dram_tensor(name, a.shape, mb.dt.from_np(a.dtype), kind="ExternalInput").ap()
            for name, a in arrays.items()]
    out = nc.dram_tensor("y", (rows, width), mb.dt.float32, kind="ExternalOutput").ap()
    bag_mlp_kernel(nc, *args, out)
    return run_bass_kernel_spmd(nc, [arrays], core_ids=[0]).results[0]["y"]
```

```python
import concourse.bass as bass
from concourse import mybir
from contextlib import ExitStack


def bag_mlp_kernel(nc: bass.Bass, x_t: bass.AP, w1_t: bass.AP, b1: bass.AP, w2_t: bass.AP, b2: bass.AP,
                   out: bass.AP):
    fp32, f32r = mybir.dt.float32, mybir.dt.float32r
    i32, fp8 = mybir.dt.int32, mybir.dt.float8e4
    ALU = mybir.AluOpType
    ACT = mybir.ActivationFunctionType

    P = 128
    M, ROWS = x_t.shape
    N, D = w1_t.shape
    C = w2_t.shape[1]
    NT = ROWS // P
    KT = -(-N // P)
    TAIL = N - (KT - 1) * P
    DC = D // P
    DROPPED = N

    ONE_BITS = 0x42600000
    STEP_BITS = 0x0C000000
    LO_WORDS = P // 4
    HI_WORDS = KT // 4
    WORDS = LO_WORDS + HI_WORDS

    BANK = 512
    BR = BANK // KT
    GR = 2 * BR
    GROUPS = -(-P // GR)
    CUTS = [0, 10, 18, 26, 34, KT]
    WCH = 5
    NWCH = KT // WCH
    STAGES = 3
    CS = [0, (C + 1) // 2, C]
    HT_COL = 320

    ctx = ExitStack()
    with ctx:
        def sb(name, shape, dt):
            return ctx.enter_context(nc.sbuf_tensor(name, shape, dt))

        def sem(name):
            return ctx.enter_context(nc.semaphore(name))

        w1_parts = sb("w1_parts", [P, KT, 2, D], f32r)
        w1_stage = sb("w1_stage", [P, STAGES, WCH, D], fp32)
        hits = sb("hits", [P, 2, KT, P], f32r)
        onehot = sb("onehot", [P, 2, P, WORDS], i32)
        x_sb = sb("x_sb", [P, ROWS], i32)
        x_wrap = sb("x_wrap", [P, 2 * P], i32)
        lo_key = sb("lo_key", [P, 2 * P], i32)
        hi_key = sb("hi_key", [P, 2 * P], i32)
        lo_bits = sb("lo_bits", [P, 2 * P], i32)
        hi_bits = sb("hi_bits", [P, 2 * P], i32)
        w2_sb = sb("w2_sb", [P, DC, C], fp32)
        b1_sb = sb("b1_sb", [P, DC], fp32)
        b2_sb = sb("b2_sb", [P, C], fp32)
        ident = sb("ident", [P, P], fp32)
        h_high = sb("h_high", [P, D], fp32)
        h_sb = sb("h_sb", [P, D], fp32)
        ht_sb = sb("ht_sb", [P, DC, P], fp32)
        y_sb = sb("y_sb", [P, 2, C], fp32)

        counts = ctx.enter_context(nc.psum_tensor("counts", [P, 2, 2, BANK], fp32))
        h_ps = ctx.enter_context(nc.psum_tensor("h_ps", [P, 2, BANK], fp32))
        y_ps = ctx.enter_context(nc.psum_tensor("y_ps", [P, 2, BANK], fp32))

        x_landed = [sem("x_first_landed"), sem("x_rest_landed")]
        w_landed = [sem(f"w_landed{s}") for s in range(STAGES)]
        tail_zeroed = sem("tail_zeroed")
        small_landed = sem("small_landed")
        ident_made = sem("ident_made")
        w_high = sem("w_high")
        w_ready = sem("w_ready")
        prep = sem("prep")
        onehot_ready = sem("onehot_ready")
        counted = sem("counted")
        hit_ready = sem("hit_ready")
        first_done = sem("first_done")
        high_copied = sem("high_copied")
        h_ready = sem("h_ready")
        ht_done = sem("ht_done")
        ht_ready = sem("ht_ready")
        y_done = sem("y_done")
        y_ready = sem("y_ready")
        stored = [sem("stored0"), sem("stored1")]

        onehot8 = onehot[:, :, :, :].bitcast(fp8)

        block = ctx.enter_context(nc.Block())

        @block.sync
        def _(sp):
            sp.dma_start(x_sb[0:M, 0:2 * P], x_t[:, 0:2 * P]).then_inc(x_landed[0], 16)
            for c in range(NWCH):
                s = c % STAGES
                if c >= STAGES:
                    sp.wait_ge(w_ready, c - STAGES + 1)
                k0 = c * WCH
                full = WCH if c < NWCH - 1 else WCH - 1
                src = w1_t[k0 * P:(k0 + full) * P, :].rearrange("(k p) d -> p k d", p=P)
                sp.dma_start(w1_stage[:, s, 0:full, :], src).then_inc(w_landed[s], 16)
                if c == NWCH - 1:
                    sp.wait_ge(tail_zeroed, 1)
                    sp.dma_start(w1_stage[0:TAIL, s, full, :], w1_t[(KT - 1) * P:N, :]).then_inc(w_landed[s], 16)
                if c == 0:
                    sp.dma_start(x_sb[0:M, 2 * P:ROWS], x_t[:, 2 * P:ROWS]).then_inc(x_landed[1], 16)
                if c == STAGES - 1:
                    sp.dma_start(w2_sb[:, :, :], w2_t.rearrange("(c p) n -> p c n", p=P)).then_inc(small_landed, 16)
                    sp.dma_start(b1_sb[:, :], b1).then_inc(small_landed, 16)
                    sp.dma_start(b2_sb[:, :], b2.rearrange("(a n) -> a n", a=1).broadcast_to([P, C])).then_inc(small_landed, 16)
            with sp.Fori(0, NT // 2) as i:
                for s in range(2):
                    sp.wait_ge(y_ready, 2 * i + s + 1)
                    sp.dma_start(out[bass.ds((2 * i + s) * P, P), :], y_sb[:, s, :]).then_inc(stored[s], 16)
            for s in range(2):
                sp.wait_ge(stored[s], 16 * (NT // 2))

        @block.gpsimd
        def _(pool):
            nc.gpsimd.memset(ident[:, :], 0.0).then_inc(ident_made, 1)
            pool.wait_ge(ident_made, 1)
            nc.gpsimd.affine_select(out=ident[:, :], in_=ident[:, :], compare_op=ALU.not_equal, fill=1.0,
                                    base=0, pattern=[[-1, P]], channel_multiplier=1).then_inc(ident_made, 1)
            pool.wait_ge(w_ready, NWCH - STAGES)
            nc.gpsimd.memset(w1_stage[:, (NWCH - 1) % STAGES, WCH - 1, :], 0.0).then_inc(tail_zeroed, 1)

        def w_arrived(eng, c):
            eng.wait_ge(w_landed[c % STAGES], 16 * (c // STAGES + 1 + (c == NWCH - 1)))

        @block.scalar
        def _(act):
            def split_high(c):
                w_arrived(act, c)
                nc.scalar.activation(w1_parts[:, c * WCH:(c + 1) * WCH, 0, :], w1_stage[:, c % STAGES, :, :],
                                     ACT.Copy).then_inc(w_high, 1)

            def make_hits(t, par, g):
                act.wait_ge(counted, t * GROUPS + g + 1)
                rows = min(GR, P - g * GR)
                if rows == GR:
                    src = counts[:, g % 2, :, 0:BR * KT].rearrange("p b (r k) -> p k b r", k=KT)
                    dst = hits[:, par, :, g * GR:(g + 1) * GR].rearrange("p k (b r) -> p k b r", b=2)
                else:
                    src = counts[:, g % 2, 0, 0:rows * KT].rearrange("p (r k) -> p k r", k=KT)
                    dst = hits[:, par, :, g * GR:P]
                nc.scalar.activation(dst, src, ACT.Sign).then_inc(hit_ready, 1)

            def copy_high(t, par):
                act.wait_ge(first_done, t + 1)
                act.wait_ge(h_ready, t)
                nc.scalar.activation(h_high[:, :], h_ps[:, par, 0:D], ACT.Copy).then_inc(high_copied, 1)

            def add_b1(t):
                act.wait_ge(ht_done, t + 1)
                for c in range(DC):
                    nc.scalar.activation(ht_sb[:, c, :], y_ps[:, c, HT_COL:HT_COL + P], ACT.Identity,
                                         bias=b1_sb[:, c:c + 1]).then_inc(ht_ready, 1)

            def tile(t, par):
                copy_high(t - 1, 1 - par)
                add_b1(t - 1)
                for g in range(GROUPS):
                    make_hits(t + 1, 1 - par, g)

            for c in range(STAGES):
                split_high(c)
            for g in range(GROUPS):
                make_hits(0, 0, g)
            for c in range(STAGES, 2 * STAGES):
                split_high(c)
            for g in range(GROUPS):
                make_hits(1, 1, g)
                if g < NWCH - 2 * STAGES:
                    split_high(2 * STAGES + g)
            act.wait_ge(small_landed, 48)
            with act.Fori(0, (NT - 2) // 2) as i:
                tile(2 * i + 1, 1)
                tile(2 * i + 2, 0)
            for t in range(NT - 2, NT):
                copy_high(t, t % 2)
                add_b1(t)

        @block.vector
        def _(dve):
            steps = 9

            def keys(pair):
                n = [0]

                def step(ins):
                    n[0] += 1
                    ins.then_inc(prep, 1)

                def sofar():
                    dve.wait_ge(prep, steps * pair + n[0])

                x = x_sb[0:M, bass.ds(pair * 2 * P, 2 * P)]
                step(nc.vector.tensor_scalar(x, x, -8192.0, 8191.0, ALU.max, ALU.min))
                sofar()
                step(nc.vector.tensor_scalar(x_wrap[0:M, :], x, 0.0, float(DROPPED + 1), ALU.is_lt, ALU.mult))
                sofar()
                step(nc.vector.scalar_tensor_tensor(x, x, 0.0, x_wrap[0:M, :], ALU.add, ALU.add))
                sofar()
                step(nc.vector.tensor_scalar(lo_bits[0:M, :], x, 26, STEP_BITS,
                                             ALU.logical_shift_left, ALU.bitwise_and))
                step(nc.vector.tensor_scalar(hi_bits[0:M, :], x, 19, STEP_BITS,
                                             ALU.logical_shift_left, ALU.bitwise_and))
                step(nc.vector.tensor_scalar(lo_key[0:M, :], x, P - 4, None, ALU.bitwise_and))
                step(nc.vector.tensor_scalar(hi_key[0:M, :], x, -4 * P, None, ALU.bitwise_and))
                sofar()
                step(nc.vector.tensor_scalar(lo_bits[0:M, :], lo_bits[0:M, :], ONE_BITS, None, ALU.bitwise_or))
                step(nc.vector.tensor_scalar(hi_bits[0:M, :], hi_bits[0:M, :], ONE_BITS, None, ALU.bitwise_or))
                sofar()
                assert n[0] == steps

            def encode(par, before=None):
                if before is not None:
                    dve.wait_ge(counted, before)
                half = slice(par * P, (par + 1) * P)
                for w in range(WORDS):
                    lo = w < LO_WORDS
                    key, bits = (lo_key, lo_bits) if lo else (hi_key, hi_bits)
                    value = 4 * w if lo else 4 * P * (w - LO_WORDS)
                    last = nc.vector.scalar_tensor_tensor(onehot[0:M, par, :, w], key[0:M, half], float(value),
                                                          bits[0:M, half].bitcast(fp32), ALU.is_equal, ALU.mult)
                last.then_inc(onehot_ready, 1)

            def split_low(c):
                w_arrived(dve, c)
                dve.wait_ge(w_high, c + 1)
                nc.vector.tensor_tensor(w1_parts[:, c * WCH:(c + 1) * WCH, 1, :], w1_stage[:, c % STAGES, :, :],
                                        w1_parts[:, c * WCH:(c + 1) * WCH, 0, :].bitcast(fp32),
                                        ALU.subtract).then_inc(w_ready, 1)

            def add_parts(t, par):
                dve.wait_ge(high_copied, t + 1)
                dve.wait_ge(ht_done, t)
                nc.vector.tensor_tensor(h_sb[:, :], h_ps[:, par, D:2 * D], h_high[:, :], ALU.add).then_inc(h_ready, 1)

            def add_b2(t, par, stores=None):
                dve.wait_ge(y_done, t + 1)
                if stores is not None:
                    dve.wait_ge(stored[par], stores)
                for c in range(2):
                    last = nc.vector.tensor_tensor(y_sb[:, par, CS[c]:CS[c + 1]], y_ps[:, c, 0:CS[c + 1] - CS[c]],
                                                   b2_sb[:, CS[c]:CS[c + 1]], ALU.add)
                last.then_inc(y_ready, 1)

            dve.wait_ge(x_landed[0], 16)
            keys(0)
            encode(0)
            for c in range(STAGES):
                split_low(c)
            encode(1)
            for c in range(STAGES, NWCH):
                split_low(c)
            dve.wait_ge(x_landed[1], 16)
            keys(1)
            encode(0, before=GROUPS)
            dve.wait_ge(small_landed, 48)
            for t in range(2):
                add_parts(t, t)
                if t == 1:
                    keys(2)
                encode(1 - t, before=(t + 2) * GROUPS)
                add_b2(t, t)
            with dve.Fori(1, (NT - 4) // 2) as i:
                add_parts(2 * i, 0)
                encode(1, before=(2 * i + 2) * GROUPS)
                add_b2(2 * i, 0, stores=16 * i)
                add_parts(2 * i + 1, 1)
                keys(i + 2)
                encode(0, before=(2 * i + 3) * GROUPS)
                add_b2(2 * i + 1, 1, stores=16 * i)
            for t in range(NT - 4, NT):
                add_parts(t, t % 2)
                if t == NT - 4:
                    encode(1, before=(t + 2) * GROUPS)
                add_b2(t, t % 2, stores=16 * (t // 2))

        @block.tensor
        def _(pe):
            def count(par, g):
                for r in range(min(GR, P - g * GR)):
                    row = g * GR + r
                    at = r % BR * KT
                    last = nc.tensor.matmul(counts[:, g % 2, r // BR, at:at + KT], onehot8[0:M, par, row, 0:P],
                                            onehot8[0:M, par, row, P:P + KT], start=True, stop=True)
                last.then_inc(counted, 1)

            def counts_read(t, g):
                if g >= 2:
                    pe.wait_ge(hit_ready, t * GROUPS + g - 1)

            def first_layer(par, k0, k1):
                for k in range(k0, k1):
                    last = nc.tensor.matmul(h_ps[:, par, :], hits[:, par, k, :],
                                            w1_parts[:, k, :, :].rearrange("p a d -> p (a d)"),
                                            start=(k == 0), stop=(k == KT - 1))
                if k1 == KT:
                    last.then_inc(first_done, 1)

            def transposes(t):
                pe.wait_ge(h_ready, t + 1)
                if not isinstance(t, int) or t > 0:
                    pe.wait_ge(y_ready, t)
                for c in range(DC):
                    last = nc.tensor.transpose(y_ps[:, c, HT_COL:HT_COL + P], h_sb[:, c * P:(c + 1) * P], ident[:, :])
                last.then_inc(ht_done, 1)

            def second_layer(t, b):
                if b == 0:
                    pe.wait_ge(ht_ready, DC * (t + 1))
                for c in range(DC):
                    last = nc.tensor.matmul(y_ps[:, b, 0:CS[b + 1] - CS[b]], ht_sb[:, c, :],
                                            w2_sb[:, c, CS[b]:CS[b + 1]], start=(c == 0), stop=(c == DC - 1))
                if b == 1:
                    last.then_inc(y_done, 1)

            def tile(t, par):
                pe.wait_ge(hit_ready, (t + 1) * GROUPS)
                pe.wait_ge(h_ready, t - 1)
                first_layer(par, CUTS[0], CUTS[1] - 1)
                pe.wait_ge(onehot_ready, t + 2)
                first_layer(par, CUTS[1] - 1, CUTS[1])
                transposes(t - 1)
                count(1 - par, 0)
                for g in range(1, GROUPS - 1):
                    counts_read(t + 1, g)
                    first_layer(par, CUTS[g], CUTS[g + 1])
                    count(1 - par, g)
                counts_read(t + 1, GROUPS - 1)
                second_layer(t - 1, 0)
                count(1 - par, GROUPS - 1)
                second_layer(t - 1, 1)

            pe.wait_ge(onehot_ready, 1)
            for g in range(GROUPS):
                counts_read(0, g)
                count(0, g)
            pe.wait_ge(hit_ready, GROUPS)
            for c in range(NWCH):
                pe.wait_ge(w_ready, c + 1)
                first_layer(0, c * WCH, (c + 1) * WCH)
                g = c - STAGES + 1
                if g == 0:
                    pe.wait_ge(onehot_ready, 2)
                if 0 <= g < GROUPS:
                    counts_read(1, g)
                    count(1, g)
            assert NWCH - STAGES + 1 >= GROUPS
            pe.wait_ge(ident_made, 2)
            with pe.Fori(0, (NT - 2) // 2) as i:
                tile(2 * i + 1, 1)
                tile(2 * i + 2, 0)
            t = NT - 1
            pe.wait_ge(hit_ready, NT * GROUPS)
            pe.wait_ge(h_ready, t - 1)
            first_layer(t % 2, 0, CUTS[1])
            transposes(t - 1)
            first_layer(t % 2, CUTS[1], CUTS[2])
            second_layer(t - 1, 0)
            second_layer(t - 1, 1)
            first_layer(t % 2, CUTS[2], KT)
            transposes(t)
            second_layer(t, 0)
            second_layer(t, 1)


def kernel(r_x, L0_rec_W1, L0_rec_b1, L0_rec_W2, L0_rec_b2):
    import numpy as np
    import concourse.bacc as bacc
    from concourse import mybir as mb
    from concourse.bass_utils import run_bass_kernel_spmd

    arrays = {
        "x_t": np.ascontiguousarray(np.asarray(r_x).T),
        "w1_t": np.ascontiguousarray(np.asarray(L0_rec_W1).T),
        "b1": np.ascontiguousarray(np.asarray(L0_rec_b1).reshape(-1, 128).T),
        "w2_t": np.ascontiguousarray(np.asarray(L0_rec_W2).T),
        "b2": np.ascontiguousarray(L0_rec_b2),
    }
    rows, width = arrays["x_t"].shape[1], arrays["w2_t"].shape[1]
    nc = bacc.Bacc("TRN2", target_bir_lowering=False, num_devices=1)
    args = [nc.dram_tensor(name, a.shape, mb.dt.from_np(a.dtype), kind="ExternalInput").ap()
            for name, a in arrays.items()]
    out = nc.dram_tensor("y", (rows, width), mb.dt.float32, kind="ExternalOutput").ap()
    bag_mlp_kernel(nc, *args, out)
    return run_bass_kernel_spmd(nc, [arrays], core_ids=[0]).results[0]["y"]
```

```python
import concourse.bass as bass
from concourse import mybir
from contextlib import ExitStack


def bag_mlp_kernel(nc: bass.Bass, x_t: bass.AP, w1_t: bass.AP, b1: bass.AP, w2_t: bass.AP, b2: bass.AP,
                   out: bass.AP):
    fp32, f32r = mybir.dt.float32, mybir.dt.float32r
    i32, bf16, fp8 = mybir.dt.int32, mybir.dt.bfloat16, mybir.dt.float8e4
    ALU = mybir.AluOpType
    ACT = mybir.ActivationFunctionType

    P = 128
    M, ROWS = x_t.shape
    N, D = w1_t.shape
    C = w2_t.shape[1]
    NT = ROWS // P
    KT = -(-N // P)
    TAIL = N - (KT - 1) * P
    DC = D // P
    DROPPED = N

    ONE_BITS = 0x42600000
    STEP_BITS = 0x0C000000
    RUN = 4
    LO_WORDS = P // 4
    HI_WORDS = KT // 4
    WORDS = LO_WORDS + HI_WORDS

    BANK = 512
    BR = BANK // KT
    GR = 2 * BR
    GROUPS = -(-P // GR)
    FIRST_ROWS = 3 * GR
    CUTS = [0, 10, 25, 37, KT]
    WCH = 4
    NWCH = KT // WCH
    STAGES = 4
    DVE_CH = NWCH - 2
    COUNT_FROM = NWCH - 1 - GROUPS
    CS = [0, (C + 1) // 2, C]
    HT_COL = 320

    ctx = ExitStack()
    with ctx:
        def sb(name, shape, dt):
            return ctx.enter_context(nc.sbuf_tensor(name, shape, dt))

        def sem(name):
            return ctx.enter_context(nc.semaphore(name))

        w1_parts = sb("w1_parts", [P, KT, 2, D], f32r)
        w1_stage = sb("w1_stage", [P, STAGES, WCH, D], fp32)
        hits = sb("hits", [P, 2, KT, P], f32r)
        onehot = sb("onehot", [P, 2, P, WORDS], i32)
        x_pair = sb("x_pair", [P, 2 * P], i32)
        key = sb("key", [P, 2, 2 * P], i32)
        bits = sb("bits", [P, 2, 2 * P], i32)
        key_run = sb("key_run", [P, 2, 2 * P, RUN], bf16)
        bits_run = sb("bits_run", [P, 2, 2 * P, RUN], bf16)
        w2_sb = sb("w2_sb", [P, DC, C], fp32)
        b1_sb = sb("b1_sb", [P, DC], fp32)
        b2_sb = sb("b2_sb", [P, C], fp32)
        ident = sb("ident", [P, P], fp32)
        h_sb = sb("h_sb", [P, D], fp32)
        ht_sb = sb("ht_sb", [P, DC, P], fp32)
        y_sb = sb("y_sb", [P, 2, C], fp32)

        counts = ctx.enter_context(nc.psum_tensor("counts", [P, 2, 2, BANK], fp32))
        h_ps = ctx.enter_context(nc.psum_tensor("h_ps", [P, 2, BANK], fp32))
        y_ps = ctx.enter_context(nc.psum_tensor("y_ps", [P, 2, BANK], fp32))

        x_landed = sem("x_landed")
        w_landed = [sem(f"w_landed{s}") for s in range(STAGES)]
        small_landed = sem("small_landed")
        tail_zeroed = sem("tail_zeroed")
        ident_made = sem("ident_made")
        w_high = sem("w_high")
        w_split = sem("w_split")
        w_split_dve = sem("w_split_dve")
        prep = sem("prep")
        keys_spread = sem("keys_spread")
        bits_spread = sem("bits_spread")
        onehot_begun = sem("onehot_begun")
        onehot_ready = sem("onehot_ready")
        counted = sem("counted")
        hit_ready = sem("hit_ready")
        first_done = sem("first_done")
        high_copied = sem("high_copied")
        h_ready = sem("h_ready")
        ht_done = sem("ht_done")
        ht_ready = sem("ht_ready")
        y_done = sem("y_done")
        y_ready = sem("y_ready")
        stored = [sem("stored0"), sem("stored1")]

        onehot8 = onehot[:, :, :, :].bitcast(fp8)

        block = ctx.enter_context(nc.Block())

        STEPS = 8

        def wait_spread(eng, pair):
            eng.wait_ge(keys_spread, RUN * (pair + 2))
            eng.wait_ge(bits_spread, 2 * (pair + 1))

        def w_arrived(eng, c):
            eng.wait_ge(w_landed[c % STAGES], 16 * (c // STAGES + 1 + (c == NWCH - 1)))

        def w_high_of(c):
            return w1_parts[:, c * WCH:(c + 1) * WCH, 0, :]

        def w_low_of(c):
            return w1_parts[:, c * WCH:(c + 1) * WCH, 1, :]

        def split_low(engine, c):
            return engine.tensor_tensor(w_low_of(c), w1_stage[:, c % STAGES, :, :], w_high_of(c).bitcast(fp32),
                                        ALU.subtract)

        def last_sums(c):
            return h_ps[:, (NT - 1 + c) % 2, 0:2 * P]

        def last_ht(c):
            return y_ps[:, 0, HT_COL:HT_COL + P] if c == 0 else h_ps[:, (NT - 1) % 2, HT_COL:HT_COL + P]

        def bits_by_run(k):
            return bits[0:M, k, :].bitcast(fp32).unsqueeze(2).broadcast_to([M, 2 * P, RUN])

        @block.sync
        def _(sp):
            def load_x(pair):
                if not isinstance(pair, int) or pair > 0:
                    sp.wait_ge(prep, STEPS * pair)
                sp.dma_start(x_pair[0:M, :], x_t[:, bass.ds(pair * 2 * P, 2 * P)]).then_inc(x_landed, 16)

            load_x(0)
            for c in range(NWCH):
                s = c % STAGES
                if c == STAGES:
                    load_x(1)
                if c >= STAGES:
                    sp.wait_ge(w_split, c - STAGES + 1)
                k0 = c * WCH
                full = WCH if c < NWCH - 1 else WCH - 1
                src = w1_t[k0 * P:(k0 + full) * P, :].rearrange("(k p) d -> p k d", p=P)
                sp.dma_start(w1_stage[:, s, 0:full, :], src).then_inc(w_landed[s], 16)
                if c == NWCH - 1:
                    sp.wait_ge(tail_zeroed, 1)
                    sp.dma_start(w1_stage[0:TAIL, s, full, :], w1_t[(KT - 1) * P:N, :]).then_inc(w_landed[s], 16)
            sp.dma_start(w2_sb[:, :, :], w2_t.rearrange("(c p) n -> p c n", p=P)).then_inc(small_landed, 16)
            sp.dma_start(b1_sb[:, :], b1).then_inc(small_landed, 16)
            sp.dma_start(b2_sb[:, :], b2.rearrange("(a n) -> a n", a=1).broadcast_to([P, C])).then_inc(small_landed, 16)

            def store(t, par):
                sp.wait_ge(y_ready, t + 1)
                sp.dma_start(out[bass.ds(t * P, P), :], y_sb[:, par, :]).then_inc(stored[par], 16)

            with sp.Fori(0, NT // 2 - 2) as i:
                load_x(i + 2)
                store(2 * i, 0)
                store(2 * i + 1, 1)
            for t in range(NT - 4, NT - 1):
                store(t, t % 2)
            t = NT - 1
            for b in range(2):
                sp.wait_ge(y_ready, t + b + 1)
                sp.dma_start(out[t * P:NT * P, CS[b]:CS[b + 1]], y_sb[:, t % 2, CS[b]:CS[b + 1]]).then_inc(stored[t % 2], 16)
            sp.wait_ge(stored[0], 16 * (NT // 2))
            sp.wait_ge(stored[1], 16 * (NT // 2 + 1))

        @block.gpsimd
        def _(pool):
            nc.gpsimd.memset(ident[:, :], 0.0).then_inc(ident_made, 1)
            pool.wait_ge(ident_made, 1)
            nc.gpsimd.affine_select(out=ident[:, :], in_=ident[:, :], compare_op=ALU.not_equal, fill=1.0,
                                    base=0, pattern=[[-1, P]], channel_multiplier=1).then_inc(ident_made, 1)
            for c in range(NWCH):
                if c == DVE_CH:
                    continue
                w_arrived(pool, c)
                pool.wait_ge(w_high, c + 1)
                split_low(nc.gpsimd, c).then_inc(w_split, 1)
                if c == NWCH - 1 - STAGES:
                    pool.wait_ge(w_split, c + 1)
                    nc.gpsimd.memset(w1_stage[:, c % STAGES, WCH - 1, :], 0.0).then_inc(tail_zeroed, 1)

        @block.scalar
        def _(act):
            def split_high(c):
                w_arrived(act, c)
                nc.scalar.activation(w_high_of(c), w1_stage[:, c % STAGES, :, :], ACT.Copy).then_inc(w_high, 1)

            def make_hits(t, par, g):
                act.wait_ge(counted, t * GROUPS + g + 1)
                rows = min(GR, P - g * GR)
                if rows == GR:
                    src = counts[:, g % 2, :, 0:BR * KT].rearrange("p b (r k) -> p k b r", k=KT)
                    dst = hits[:, par, :, g * GR:(g + 1) * GR].rearrange("p k (b r) -> p k b r", b=2)
                else:
                    src = counts[:, g % 2, 0, 0:rows * KT].rearrange("p (r k) -> p k r", k=KT)
                    dst = hits[:, par, :, g * GR:P]
                nc.scalar.activation(dst, src, ACT.Sign).then_inc(hit_ready, 1)

            def copy_high(t, par):
                act.wait_ge(first_done, t + 1)
                nc.scalar.activation(h_sb[:, :], h_ps[:, par, 0:D], ACT.Copy).then_inc(high_copied, 1)

            def spread_keys(pair, rows=slice(0, 2 * P)):
                act.wait_ge(prep, STEPS * (pair + 1))
                if not isinstance(pair, int) or pair > 0:
                    act.wait_ge(onehot_ready, 2 * pair)
                for j in range(RUN):
                    nc.scalar.activation(key_run[0:M, :, rows, j], key[0:M, :, rows], ACT.Copy,
                                         bias=-4.0 * j).then_inc(keys_spread, 1)

            def spread_bits():
                for k in range(2):
                    nc.scalar.activation(bits_run[0:M, k, :, :], bits_by_run(k), ACT.Copy).then_inc(bits_spread, 1)

            def add_b1(t):
                act.wait_ge(ht_done, t + 1)
                for c in range(DC):
                    nc.scalar.activation(ht_sb[:, c, :], y_ps[:, c, HT_COL:HT_COL + P], ACT.Identity,
                                         bias=b1_sb[:, c:c + 1]).then_inc(ht_ready, 1)

            split_high(0)
            spread_keys(0, rows=slice(0, P))
            split_high(1)
            spread_keys(0, rows=slice(P, 2 * P))
            for c in range(2, 5):
                split_high(c)
            for g in range(GROUPS):
                make_hits(0, 0, g)
            for c in range(5, NWCH - 1):
                split_high(c)
            make_hits(1, 1, 0)
            spread_keys(1)
            make_hits(1, 1, 1)
            split_high(NWCH - 1)
            for g in range(2, GROUPS):
                make_hits(1, 1, g)
            act.wait_ge(small_landed, 48)
            def odd_tile(i, more=True):
                copy_high(2 * i, 0)
                add_b1(2 * i)
                for g in range(GROUPS):
                    make_hits(2 * i + 2, 0, g)
                    if more and g == 3:
                        spread_keys(i + 2)

            def even_tile(i, more=True):
                copy_high(2 * i + 1, 1)
                if more:
                    spread_bits()
                add_b1(2 * i + 1)
                for g in range(GROUPS):
                    make_hits(2 * i + 3, 1, g)

            with act.Fori(0, NT // 2 - 2) as i:
                odd_tile(i)
                even_tile(i)
            odd_tile(NT // 2 - 2, more=False)
            even_tile(NT // 2 - 2, more=False)
            copy_high(NT - 2, (NT - 2) % 2)
            add_b1(NT - 2)
            t = NT - 1
            for c in range(DC):
                act.wait_ge(first_done, t + c + 1)
                nc.scalar.activation(h_sb[:, c * P:(c + 1) * P], last_sums(c)[:, 0:P], ACT.Copy).then_inc(high_copied, 1)
                act.wait_ge(ht_done, t + c + 1)
                nc.scalar.activation(ht_sb[:, c, :], last_ht(c), ACT.Identity,
                                     bias=b1_sb[:, c:c + 1]).then_inc(ht_ready, 1)

        @block.vector
        def _(dve):
            def keys(pair):
                n = [0]

                def step(ins):
                    n[0] += 1
                    ins.then_inc(prep, 1)

                def sofar():
                    dve.wait_ge(prep, STEPS * pair + n[0])

                x, wrap = x_pair[0:M, :], key[0:M, 0, :]
                dve.wait_ge(x_landed, 16 * (pair + 1))
                if not isinstance(pair, int) or pair > 0:
                    wait_spread(dve, pair - 1)
                step(nc.vector.tensor_scalar(x, x, -8192.0, 8191.0, ALU.max, ALU.min))
                sofar()
                step(nc.vector.tensor_scalar(wrap, x, 0.0, float(DROPPED + 1), ALU.is_lt, ALU.mult))
                sofar()
                step(nc.vector.scalar_tensor_tensor(x, x, 0.0, wrap, ALU.add, ALU.add))
                sofar()
                step(nc.vector.tensor_scalar(key[0:M, 0, :], x, P - 4, None, ALU.bitwise_and))
                step(nc.vector.tensor_scalar(key[0:M, 1, :], x, 7, -4, ALU.arith_shift_right, ALU.bitwise_and))
                step(nc.vector.tensor_scalar(bits[0:M, 0, :], x, 26, STEP_BITS,
                                             ALU.logical_shift_left, ALU.bitwise_and))
                step(nc.vector.tensor_scalar(bits[0:M, 1, :], x, 19, STEP_BITS,
                                             ALU.logical_shift_left, ALU.bitwise_and))
                sofar()
                step(nc.vector.tensor_scalar(bits[0:M, :, :], bits[0:M, :, :], ONE_BITS, None, ALU.bitwise_or))
                assert n[0] == STEPS

            def encode(pair, par, before=None, r0=0, r1=P):
                if isinstance(pair, int) and pair == par == 0:
                    dve.wait_ge(keys_spread, RUN)
                    dve.wait_ge(bits_spread, 2)
                else:
                    wait_spread(dve, pair)
                if before is not None:
                    dve.wait_ge(counted, before)
                rows = slice(par * P + r0, par * P + r1)
                for k, first, words in ((0, 0, LO_WORDS), (1, LO_WORDS, HI_WORDS)):
                    for w in range(0, words, RUN):
                        n = min(RUN, words - w)
                        last = nc.vector.scalar_tensor_tensor(onehot[0:M, par, r0:r1, first + w:first + w + n],
                                                              key_run[0:M, k, rows, 0:n], 4.0 * w,
                                                              bits_run[0:M, k, rows, 0:n], ALU.is_equal, ALU.mult)
                last.then_inc(onehot_ready if r1 == P else onehot_begun, 1)

            def add_parts(t, par):
                dve.wait_ge(high_copied, t + 1)
                nc.vector.tensor_tensor(h_sb[:, :], h_ps[:, par, D:2 * D], h_sb[:, :], ALU.add).then_inc(h_ready, 1)

            def add_b2(t, par, stores=None, by_bank=False):
                if stores is not None:
                    dve.wait_ge(stored[par], stores)
                for c in range(2):
                    dve.wait_ge(y_done, 2 * t + c + 1)
                    last = nc.vector.tensor_tensor(y_sb[:, par, CS[c]:CS[c + 1]], y_ps[:, c, 0:CS[c + 1] - CS[c]],
                                                   b2_sb[:, CS[c]:CS[c + 1]], ALU.add)
                    if c == 1 or by_bank:
                        last.then_inc(y_ready, 1)

            def spread_bits(pair):
                dve.wait_ge(prep, STEPS * (pair + 1))
                for k in range(2):
                    nc.vector.tensor_copy(bits_run[0:M, k, :, :], bits_by_run(k)).then_inc(bits_spread, 1)

            keys(0)
            spread_bits(0)
            encode(0, 0, r1=FIRST_ROWS)
            encode(0, 0, r0=FIRST_ROWS)
            encode(0, 1)
            keys(1)
            dve.wait_ge(onehot_ready, 2)
            spread_bits(1)
            w_arrived(dve, DVE_CH)
            dve.wait_ge(w_high, DVE_CH + 1)
            split_low(nc.vector, DVE_CH).then_inc(w_split_dve, 1)
            encode(1, 0, before=GROUPS)
            dve.wait_ge(small_landed, 48)
            add_parts(0, 0)
            encode(1, 1, before=2 * GROUPS)
            keys(2)
            add_b2(0, 0)
            add_parts(1, 1)
            encode(2, 0, before=3 * GROUPS)
            add_b2(1, 1)
            with dve.Fori(1, NT // 2 - 2) as i:
                add_parts(2 * i, 0)
                encode(i + 1, 1, before=(2 * i + 2) * GROUPS)
                keys(i + 2)
                add_b2(2 * i, 0, stores=16 * i)
                add_parts(2 * i + 1, 1)
                encode(i + 2, 0, before=(2 * i + 3) * GROUPS)
                add_b2(2 * i + 1, 1, stores=16 * i)
            for t in range(NT - 4, NT - 1):
                add_parts(t, t % 2)
                if t == NT - 4:
                    encode(NT // 2 - 1, 1, before=(t + 2) * GROUPS)
                add_b2(t, t % 2, stores=16 * (t // 2))
            t = NT - 1
            for c in range(DC):
                half = h_sb[:, c * P:(c + 1) * P]
                dve.wait_ge(high_copied, t + c + 1)
                nc.vector.tensor_tensor(half, last_sums(c)[:, P:2 * P], half, ALU.add).then_inc(h_ready, 1)
            add_b2(t, t % 2, stores=16 * (t // 2), by_bank=True)

        @block.tensor
        def _(pe):
            def count(par, g):
                for r in range(min(GR, P - g * GR)):
                    row = g * GR + r
                    at = r % BR * KT
                    last = nc.tensor.matmul(counts[:, g % 2, r // BR, at:at + KT], onehot8[0:M, par, row, 0:P],
                                            onehot8[0:M, par, row, P:P + KT], start=True, stop=True)
                last.then_inc(counted, 1)

            def counts_read(t, g):
                if g >= 2:
                    pe.wait_ge(hit_ready, t * GROUPS + g - 1)

            def first_layer(par, k0, k1):
                for k in range(k0, k1):
                    last = nc.tensor.matmul(h_ps[:, par, :], hits[:, par, k, :],
                                            w1_parts[:, k, :, :].rearrange("p a d -> p (a d)"),
                                            start=(k == 0), stop=(k == KT - 1))
                if k1 == KT:
                    last.then_inc(first_done, 1)

            def transposes(t):
                pe.wait_ge(h_ready, t + 1)
                if not isinstance(t, int) or t > 0:
                    pe.wait_ge(y_ready, t)
                for c in range(DC):
                    last = nc.tensor.transpose(y_ps[:, c, HT_COL:HT_COL + P], h_sb[:, c * P:(c + 1) * P], ident[:, :])
                last.then_inc(ht_done, 1)

            def second_layer(t, b):
                if b == 0:
                    pe.wait_ge(ht_ready, DC * (t + 1))
                for c in range(DC):
                    last = nc.tensor.matmul(y_ps[:, b, 0:CS[b + 1] - CS[b]], ht_sb[:, c, :],
                                            w2_sb[:, c, CS[b]:CS[b + 1]], start=(c == 0), stop=(c == DC - 1))
                last.then_inc(y_done, 1)

            def tile(t, par):
                pe.wait_ge(hit_ready, (t + 1) * GROUPS)
                for p in range(GROUPS // 2):
                    cut = CUTS[p + 1]
                    first_layer(par, CUTS[p], cut - 1)
                    if p == 0:
                        pe.wait_ge(onehot_ready, t + 2)
                    else:
                        pe.wait_ge(hit_ready, (t + 1) * GROUPS + 2 * p)
                    first_layer(par, cut - 1, cut)
                    if p == 0:
                        transposes(t - 1)
                    count(1 - par, 2 * p)
                    count(1 - par, 2 * p + 1)
                first_layer(par, cut, KT)
                second_layer(t - 1, 0)
                second_layer(t - 1, 1)

            def first_half(c, k0, k1):
                for k in range(k0, k1):
                    last = nc.tensor.matmul(last_sums(c), hits[:, (NT - 1) % 2, k, :],
                                            w1_parts[:, k, :, c * P:(c + 1) * P], start=(k == 0), stop=(k == KT - 1))
                if k1 == KT:
                    last.then_inc(first_done, 1)

            def last_transpose(c):
                pe.wait_ge(h_ready, NT + c)
                if c == 0:
                    pe.wait_ge(y_ready, NT - 1)
                nc.tensor.transpose(last_ht(c), h_sb[:, c * P:(c + 1) * P], ident[:, :]).then_inc(ht_done, 1)

            def last_second(c):
                pe.wait_ge(ht_ready, DC * (NT - 1) + c + 1)
                for b in range(2):
                    last = nc.tensor.matmul(y_ps[:, b, 0:CS[b + 1] - CS[b]], ht_sb[:, c, :],
                                            w2_sb[:, c, CS[b]:CS[b + 1]], start=(c == 0), stop=(c == DC - 1))
                    if c == DC - 1:
                        last.then_inc(y_done, 1)

            def keep_warm(n):
                for _ in range(n):
                    nc.tensor.matmul(h_ps[:, 1, 0:P], ident[:, :], ident[:, :], start=True, stop=True)

            pe.wait_ge(ident_made, 2)
            pe.wait_ge(keys_spread, RUN)
            keep_warm(8)
            pe.wait_ge(onehot_begun, 1)
            for g in range(GROUPS):
                if g == FIRST_ROWS // GR:
                    pe.wait_ge(onehot_ready, 1)
                counts_read(0, g)
                count(0, g)
                keep_warm(1)
            pe.wait_ge(hit_ready, GROUPS)
            for c in range(NWCH):
                if c == DVE_CH:
                    pe.wait_ge(w_split_dve, 1)
                else:
                    pe.wait_ge(w_split, c + 1 - (c > DVE_CH))
                first_layer(0, c * WCH, (c + 1) * WCH)
                g = c - COUNT_FROM
                if g == 0:
                    pe.wait_ge(onehot_ready, 2)
                if 0 <= g < GROUPS:
                    counts_read(1, g)
                    count(1, g)
            tile(1, 1)
            with pe.Fori(1, NT // 2 - 1) as i:
                tile(2 * i, 0)
                tile(2 * i + 1, 1)
            tile(NT - 2, 0)
            t = NT - 1
            pe.wait_ge(hit_ready, NT * GROUPS)
            first_half(0, 0, KT // 2)
            transposes(t - 1)
            first_half(0, KT // 2, KT - 4)
            second_layer(t - 1, 0)
            second_layer(t - 1, 1)
            first_half(0, KT - 4, KT)
            first_half(1, 0, KT // 2)
            last_transpose(0)
            first_half(1, KT // 2, KT)
            last_second(0)
            last_transpose(1)
            last_second(1)


def kernel(r_x, L0_rec_W1, L0_rec_b1, L0_rec_W2, L0_rec_b2):
    import numpy as np
    import concourse.bacc as bacc
    from concourse import mybir as mb
    from concourse.bass_utils import run_bass_kernel_spmd

    arrays = {
        "x_t": np.ascontiguousarray(np.asarray(r_x).T),
        "w1_t": np.ascontiguousarray(np.asarray(L0_rec_W1).T),
        "b1": np.ascontiguousarray(np.asarray(L0_rec_b1).reshape(-1, 128).T),
        "w2_t": np.ascontiguousarray(np.asarray(L0_rec_W2).T),
        "b2": np.ascontiguousarray(L0_rec_b2),
    }
    rows, width = arrays["x_t"].shape[1], arrays["w2_t"].shape[1]
    nc = bacc.Bacc("TRN2", target_bir_lowering=False, num_devices=1)
    args = [nc.dram_tensor(name, a.shape, mb.dt.from_np(a.dtype), kind="ExternalInput").ap()
            for name, a in arrays.items()]
    out = nc.dram_tensor("y", (rows, width), mb.dt.float32, kind="ExternalOutput").ap()
    bag_mlp_kernel(nc, *args, out)
    return run_bass_kernel_spmd(nc, [arrays], core_ids=[0]).results[0]["y"]
```
